# Optimizing a Trainium2 kernel written in Bass

```python
import numpy as np
import jax
import jax.numpy as jnp

def _softmax(x, axis=-1):
    return jax.nn.softmax(x, axis=axis)

def _gelu(x):
    return jax.nn.gelu(x, approximate=True)

def _silu(x):
    return jax.nn.silu(x)

def _sigmoid(x):
    return jax.nn.sigmoid(x)

def _layernorm(x, axis=-1, eps=1e-05):
    m = jnp.mean(x, axis=axis, keepdims=True)
    v = jnp.var(x, axis=axis, keepdims=True)
    return (x - m) / jnp.sqrt(v + eps)

def _scatter_add(tgt, idx, src, axis=0):
    return tgt.at[idx].add(src)

def _segment_sum(src, seg, n):
    return jax.ops.segment_sum(src, seg, n)
kernel_name = 'mk_gnn_ffn_d1_gnn_r8_59316b'

def setup_inputs(seed: int=0):
    np.random.seed(seed)
    _w = jnp.asarray

    def _rec_inputs():
        import jax
        import jax.numpy as jnp
        _gk = jax.random.key(seed)
        x = -0.0003713 + 1 * jax.random.normal(jax.random.fold_in(_gk, 1), (6250, 256), jnp.float32)
        src = jax.random.randint(jax.random.fold_in(_gk, 2), (200000,), 0, 6250, jnp.int32)
        dst = jnp.minimum((6250 * jax.random.uniform(jax.random.fold_in(_gk, 3), (200000,)) ** 2.0).astype(jnp.int32), 49999)
        _o = jnp.argsort(dst, stable=True)
        src = src[_o]
        dst = dst[_o]
        return (x, src, dst)
    x, src, dst = _rec_inputs()

    def _L0_gnn_setup():
        import jax, jax.numpy as jnp
        import numpy as np
        N = 6250
        E = 100000
        IN_DIM = 256
        D = 32
        H = 8
        NEG_SLOPE = 0.01
        key = jax.random.key(seed)
        k1, k2, k3, k4, k5 = jax.random.split(key, 5)
        h = jax.random.normal(k1, (N, IN_DIM), dtype=jnp.float32)
        W = jax.random.normal(k2, (H, IN_DIM, D), dtype=jnp.float32) * 0.05
        attn_w = jax.random.normal(k3, (H, 2 * D), dtype=jnp.float32) * 0.05
        src = jax.random.randint(k4, (E,), 0, N, dtype=jnp.int64)
        dst = jax.random.randint(k5, (E,), 0, N, dtype=jnp.int64)
        return {'h': h, 'W': W, 'attn_w': attn_w, 'src': src, 'dst': dst}
    _L0_gnn_all = _L0_gnn_setup()
    _L0_gnn_in = {k: v for k, v in _L0_gnn_all.items() if k in ('W', 'attn_w')}
    del _L0_gnn_all

    def _L0_ffn_setup():
        import math
        import jax, jax.numpy as jnp
        import numpy as np
        CAPACITY_FACTOR = 1.25
        TOP_K = 2
        LN_EPS = 1e-05

        def _layer_norm(x, gamma, beta):
            mu = jnp.mean(x, axis=-1, keepdims=True)
            var = jnp.var(x, axis=-1, keepdims=True)
            return (x - mu) * jax.lax.rsqrt(var + LN_EPS) * gamma + beta
        key = jax.random.key(seed)
        ks = jax.random.split(key, 4)
        B, S, D, F, E = (8, 512, 256, 512, 8)
        x = jax.random.normal(ks[0], (B, S, D), dtype=jnp.float32)
        Wr = jax.random.normal(ks[1], (D, E), dtype=jnp.float32) / np.sqrt(D)
        br = jnp.zeros((E,), jnp.float32)
        W1 = jax.random.normal(ks[2], (E, D, F), dtype=jnp.float32) / np.sqrt(D)
        b1 = jnp.zeros((E, F), jnp.float32)
        W2 = jax.random.normal(ks[3], (E, F, D), dtype=jnp.float32) / np.sqrt(F)
        b2 = jnp.zeros((E, D), jnp.float32)
        gamma = jnp.ones((D,), jnp.float32)
        beta = jnp.zeros((D,), jnp.float32)
        return {'x': x, 'Wr': Wr, 'br': br, 'W1': W1, 'b1': b1, 'W2': W2, 'b2': b2, 'gamma': gamma, 'beta': beta}
    _L0_ffn_all = _L0_ffn_setup()
    _L0_ffn_in = {k: v for k, v in _L0_ffn_all.items() if k in ('Wr', 'br', 'W1', 'b1', 'W2', 'b2', 'gamma', 'beta')}
    del _L0_ffn_all
    return {'x': x, 'src': src, 'dst': dst, 'L0_gnn_W': _L0_gnn_in['W'], 'L0_gnn_attn_w': _L0_gnn_in['attn_w'], 'L0_ffn_Wr': _L0_ffn_in['Wr'], 'L0_ffn_br': _L0_ffn_in['br'], 'L0_ffn_W1': _L0_ffn_in['W1'], 'L0_ffn_b1': _L0_ffn_in['b1'], 'L0_ffn_W2': _L0_ffn_in['W2'], 'L0_ffn_b2': _L0_ffn_in['b2'], 'L0_ffn_gamma': _L0_ffn_in['gamma'], 'L0_ffn_beta': _L0_ffn_in['beta']}

def reference(x, src, dst, L0_gnn_W, L0_gnn_attn_w, L0_ffn_Wr, L0_ffn_br, L0_ffn_W1, L0_ffn_b1, L0_ffn_W2, L0_ffn_b2, L0_ffn_gamma, L0_ffn_beta):
    import jax
    import jax.numpy as jnp

    def _L0_gnn_ref(h, W, attn_w, src, dst):
        import jax, jax.numpy as jnp
        import numpy as np
        N = 6250
        E = 100000
        IN_DIM = 256
        D = 32
        H = 8
        NEG_SLOPE = 0.01
        z = jnp.einsum('ni,hid->nhd', h, W)
        a_l, a_r = (attn_w[:, :D], attn_w[:, D:])
        el = jnp.einsum('nhd,hd->nh', z, a_l)
        er = jnp.einsum('nhd,hd->nh', z, a_r)
        e = jax.nn.leaky_relu(el[src] + er[dst], NEG_SLOPE)
        m = jax.ops.segment_max(e, dst, num_segments=N)
        m = jnp.where(jnp.isfinite(m), m, 0.0)
        num = jnp.exp(e - m[dst])
        den = jax.ops.segment_sum(num, dst, num_segments=N)
        den_e = den[dst]
        alpha = num / jnp.where(den_e > 0, den_e, 1.0)
        msg = alpha[:, :, None] * z[src]
        hout = jax.ops.segment_sum(msg, dst, num_segments=N)
        return hout.reshape(N, H * D)

    def _L0_ffn_ref(x, Wr, br, W1, b1, W2, b2, gamma, beta):
        import math
        import jax, jax.numpy as jnp
        import numpy as np
        CAPACITY_FACTOR = 1.25
        TOP_K = 2
        LN_EPS = 1e-05

        def _layer_norm(x, gamma, beta):
            mu = jnp.mean(x, axis=-1, keepdims=True)
            var = jnp.var(x, axis=-1, keepdims=True)
            return (x - mu) * jax.lax.rsqrt(var + LN_EPS) * gamma + beta
        B, S, D = x.shape
        E = Wr.shape[1]
        N = B * S
        K = TOP_K
        logits = jnp.mean(x, axis=1) @ Wr + br
        routing_weights = jax.nn.softmax(logits, axis=-1)
        capacity = float(math.ceil(N * CAPACITY_FACTOR / E))
        expected_loads = routing_weights.sum(axis=0) * (N / B)
        scale = jnp.where(expected_loads > capacity, capacity / expected_loads, 1.0)
        routing_weights = jax.nn.softmax(routing_weights * scale, axis=-1)
        rw_tok = jnp.broadcast_to(routing_weights[:, None, :], (B, S, E)).reshape(N, E)
        top_w, top_i = jax.lax.top_k(rw_tok, K)
        top_w = jax.nn.softmax(top_w, axis=-1)
        xf = x.reshape(N, D)
        h = jax.nn.gelu(jnp.einsum('nd,edf->enf', xf, W1) + b1[:, None, :], approximate=False)
        y = jnp.einsum('enf,efd->end', h, W2) + b2[:, None, :]
        w_dense = jnp.zeros((N, E), x.dtype).at[jnp.arange(N)[:, None], top_i].add(top_w)
        out = jnp.einsum('ne,end->nd', w_dense, y).reshape(B, S, D)
        out = _layer_norm(out + x, gamma, beta)
        return out
    x = x + _L0_gnn_ref(_layernorm(x, axis=-1), L0_gnn_W, L0_gnn_attn_w, src, dst)
    x = x + _L0_ffn_ref(_layernorm(x, axis=-1)[None], L0_ffn_Wr, L0_ffn_br, L0_ffn_W1, L0_ffn_b1, L0_ffn_W2, L0_ffn_b2, L0_ffn_gamma, L0_ffn_beta)[0]
    return x

_drawn_inputs = setup_inputs


def setup_inputs(seed=0):
    import zlib

    import numpy as np

    out = dict(_drawn_inputs(seed))
    spreads = {'L0_ffn_br': (0.0, 0.1),
     'L0_ffn_b1': (0.0, 0.374),
     'L0_ffn_b2': (0.0, 0.1),
     'L0_ffn_gamma': (1.0, 0.2),
     'L0_ffn_beta': (0.0, 0.1)}
    factors = {'L0_ffn_Wr': 8.0}
    for name, (base, spread) in spreads.items():
        noise = np.random.default_rng([zlib.crc32(name.encode()), seed]).standard_normal(out[name].shape)
        drawn = base * np.exp(spread * noise) if base else spread * noise
        out[name] = jnp.asarray(drawn.astype(out[name].dtype))
    for name, factor in factors.items():
        out[name] = (out[name] * factor).astype(out[name].dtype)
    return out
```

```python
from contextlib import ExitStack

import concourse.bass as bass
from concourse import mybir

F32 = mybir.dt.float32
BF16 = mybir.dt.bfloat16
I32 = mybir.dt.int32
ALU = mybir.AluOpType
ACT = mybir.ActivationFunctionType
AX = mybir.AxisListType

P = 128
N = 6250
D = 256
KD = D // P
H = 8
HD = D // H
NB = 50
NODES = NB * P
LASTB = (N - 1) // P
TAIL = N - LASTB * P
E = 200000
TPG = 4
GE = TPG * P
G = -(-E // GE)
ROW = D + H
U = 8
STEPS = -(-(G + LASTB) // U) * U
SP_LEN = STEPS + U
SLOPE = 0.01
LN_EPS = 1e-5
NE = 8
FF = 512
FC = FF // P
TOPK = 2
CAP = float(-(-(N * 5) // (4 * NE)))
CH = 2
NCH = NB // CH
LAGS_MAX = 4


def build(nc, x, src, dst, gnn_w, attn_w, wr, br, w1, b1, w2, b2, gamma, beta, table, out):
    with ExitStack() as ctx:
        def sb(name, shape, dt=F32):
            return ctx.enter_context(nc.sbuf_tensor(name, shape, dt))

        def sem(name):
            return ctx.enter_context(nc.semaphore(name))

        bank = [ctx.enter_context(nc.psum_tensor(f"bank{i}", [P, 512], F32)) for i in range(8)]

        X = sb("X", [P, NB, D])
        A = sb("A", [P, NB, ROW])
        T = sb("T", [P, KD * NODES])
        ident = sb("ident", [P, P])
        identb = sb("identb", [P, P], BF16)
        ones = sb("ones", [P, P])
        neghalf = sb("neghalf", [P, 1])
        small = sb("small", [P, 2, 16])
        Wz = sb("Wz", [P, KD, D + 2 * H])
        Hn = sb("Hn", [P, 2, D])
        HT = sb("HT", [P, 2, KD, P])
        elmax = sb("elmax", [P, 2, H])
        erc3 = sb("erc3", [P, NB, 3, 2 * H], BF16)
        blockbase = sb("blockbase", [P, NB])
        iota = sb("iota", [P, P], BF16)
        firsts = sb("firsts", [P, 4], I32)
        gidx = sb("gidx", [P, 4], I32)
        pathf = sb("pathf", [P, 4])
        onesb = sb("onesb", [P, 1], BF16)
        stepg = sb("stepg", [1, 2, SP_LEN], I32)
        idx = sb("idx", [P, U * TPG], I32)
        dloc = sb("dloc", [P, 2, TPG])
        logit = sb("logit", [P, 2, 4, TPG * H])
        fblk = sb("fblk", [P, 4], I32)
        rank = sb("rank", [1, NE])
        rden = sb("rden", [P, NB, H])
        meanT = sb("meanT", [P, KD])
        Wr = sb("Wr", [P, KD, NE])
        r8 = sb("r8", [1, 24, NE])
        topi = sb("topi", [1, TOPK], I32)
        wcol = sb("wcol", [P, TOPK])
        b1c = sb("b1c", [P, TOPK, FC])
        b2all = sb("b2all", [P, D])
        gam = sb("gam", [P, D])
        bet = sb("bet", [P, D])

        gath = T[:, 0:U * TPG * ROW].rearrange("p (u j c) -> p u j c", u=U, c=ROW)
        at = [U * TPG * ROW]

        def carve(arena, at, width, shape, dt=F32):
            v = arena[:, at[0]:at[0] + width]
            at[0] += width
            if dt != F32:
                v = v.bitcast(dt)
            if len(shape) == 1:
                return v
            names = "abcd"[:len(shape)]
            return v.rearrange(f"p ({' '.join(names)}) -> p {' '.join(names)}", **dict(zip(names, shape)))

        OHf = carve(T, at, 4 * TPG * P, (4, TPG, P))
        OHb = carve(T, at, TPG * P, (2, TPG, P), BF16)
        OHT = carve(T, at, TPG * P, (2, TPG, P), BF16)
        passed = carve(T, at, 2 * SP_LEN, (4, SP_LEN), BF16)
        weights = sb("weights", [P, 2 * TOPK * KD * FF])
        W1 = weights[:, 0:TOPK * KD * FF].rearrange("p (t k f) -> p t k f", t=TOPK, k=KD)
        W2 = weights[:, TOPK * KD * FF:].rearrange("p (t c d) -> p t c d", t=TOPK, c=FC)
        at = [0]
        ab = carve(weights, at, 2 * D, (2 * D,))
        wprod = carve(weights, at, D, (D,))
        steps = carve(weights, at, SP_LEN, (SP_LEN,))
        stepf = carve(weights, at, 2 * SP_LEN, (2, SP_LEN))
        ee = carve(weights, at, NB * 2 * H, (NB, 2 * H))
        res = carve(weights, at, NB * 2 * H, (NB, 2 * H))
        hidden = sb("hidden", [P, 2 * TOPK * FC * CH * P])
        hid = hidden[:, :].rearrange("p (s n c) -> p s n c", s=2, n=TOPK * FC)
        at = [0]
        srcs = carve(hidden, at, G * TPG, (G * TPG,), I32)
        dsts = carve(hidden, at, G * TPG, (G * TPG,), I32)
        erc = carve(hidden, at, NB * 2 * H, (NB, 2 * H))
        b2row = hidden[0:1, 0:TOPK * D].rearrange("p (t d) -> p t d", t=TOPK)
        b2mix = hidden[0:1, TOPK * D:2 * TOPK * D].rearrange("p (t d) -> p t d", t=TOPK)
        fo = HT[:, :, :, :].rearrange("p s k n -> p s (k n)")
        rbuf = Hn
        XT = T[:, :].rearrange("p (k n) -> p k n", k=KD)

        s_in = sem("s_in")
        s_x = sem("s_x")
        s_edges = sem("s_edges")
        s_ab = sem("s_ab")
        s_const = sem("s_const")
        s_iden = sem("s_iden")
        s_held = sem("s_held")
        s_v = sem("s_v")
        s_wz = sem("s_wz")
        s_h = sem("s_h")
        s_st = sem("s_st")
        s_hT = sem("s_hT")
        s_hTc = sem("s_hTc")
        s_z = sem("s_z")
        s_zc = sem("s_zc")
        s_ec = sem("s_ec")
        s_tab = sem("s_tab")
        s_elm = sem("s_elm")
        s_gmax = sem("s_gmax")
        s_erc = sem("s_erc")
        s_pass = sem("s_pass")
        s_cnt = sem("s_cnt")
        s_plan = sem("s_plan")
        s_zero = sem("s_zero")
        e_idx = sem("e_idx")
        e_gath = [sem(f"e_gath{u}") for u in range(U)]
        e_dl = sem("e_dl")
        e_oh = sem("e_oh")
        e_tp = sem("e_tp")
        e_ohT = sem("e_ohT")
        e_ohf = sem("e_ohf")
        e_er = sem("e_er")
        e_l1 = sem("e_l1")
        e_l2 = sem("e_l2")
        e_l3 = sem("e_l3")
        e_lg = sem("e_lg")
        e_num = sem("e_num")
        e_msg = sem("e_msg")
        e_sc = sem("e_sc")
        e_acc = sem("e_acc")
        n_d = sem("n_d")
        n_hout = sem("n_hout")
        n_x1 = sem("n_x1")
        n_st = sem("n_st")
        s_rs = sem("s_rs")
        n_rs = sem("n_rs")
        f_rs = sem("f_rs")
        n_bias = sem("n_bias")
        n_xn = sem("n_xn")
        n_keep = sem("n_keep")
        n_tp = sem("n_tp")
        n_xT = sem("n_xT")
        r_mean = sem("r_mean")
        r_v = sem("r_v")
        r_pe = sem("r_pe")
        r_act = sem("r_act")
        r_exp = sem("r_exp")
        r_wrow = sem("r_wrow")
        r_b2 = sem("r_b2")
        r_top = sem("r_top")
        r_w = sem("r_w")
        r_gb = sem("r_gb")
        r_ready = sem("r_ready")
        f_h = sem("f_h")
        f_g = sem("f_g")
        f_y = sem("f_y")
        f_r = sem("f_r")
        f_b = sem("f_b")
        f_st = sem("f_st")
        f_o = sem("f_o")
        f_out = [sem(f"f_out{i}") for i in range(2)]

        def pipeline(eng, count, unroll, lags, body):
            peeled = -(-LAGS_MAX // unroll)
            for s in range(peeled * unroll):
                body(s, s % unroll, s // unroll, lambda lag, s=s: s >= lag)
            with eng.Fori(peeled, count // unroll) as i:
                for u in range(unroll):
                    body(i * unroll + u, u, i, lambda lag: True)
            for s in range(count, count + lags):
                body(s, s % unroll, s // unroll, lambda lag, s=s: lag > s - count)

        def chunks(eng, body, lags=0):
            for s in range(3):
                body(s, s, lambda lag, s=s: s >= lag)
            with eng.Fori(0, (NCH - 3) // 2) as i:
                for u in range(2):
                    body(i * 2 + (3 + u), 3 + u, lambda lag: True)
            for s in range(NCH, NCH + lags):
                body(s, s, lambda lag, s=s: lag > s - NCH)

        def blk(t, b, lo=0, hi=D):
            return t[:, bass.ds(b, 1), lo:hi].rearrange("p a d -> p (a d)")

        LA = 4
        psT = [bank[v][:, :].bitcast(BF16)[:, 0:TPG * P].rearrange("p (j e) -> p j e", j=TPG) for v in range(2)]
        psE = [bank[2 + v][:, 0:TPG * 2 * H].rearrange("p (j c) -> p j c", j=TPG) for v in range(2)]
        psA = [bank[4 + v][:, 0:ROW] for v in range(2)]
        STORES = 5
        SB_ = NB // STORES

        block = ctx.enter_context(nc.Block())

        @block.sync
        def _(sp):
            xv = x.rearrange("(b p) d -> p b d", p=P)
            for k in range(KD):
                sp.dma_start(Wz[:, k, 0:D].rearrange("p (h d) -> p h d", h=H),
                             gnn_w[:, k * P:(k + 1) * P, :].rearrange("h p d -> p h d")).then_inc(s_in, 16)
            for c in range(STORES):
                sp.dma_start(X[:, c * SB_:(c + 1) * SB_, :], xv[:, c * SB_:(c + 1) * SB_, :]).then_inc(s_x, 16)
            tv = table.rearrange("(b p) c -> p b c", p=P)
            for c in range(STORES):
                sp.wait_ge(s_zc, (c + 1) * SB_)
                sp.dma_start(tv[:, c * SB_:(c + 1) * SB_, :], A[:, c * SB_:(c + 1) * SB_, :]).then_inc(s_tab, 16)
            sp.wait_ge(s_tab, STORES * 16)
            sp.wait_ge(r_top, 1)
            for k in range(TOPK):
                e = sp.value_load(topi[0:1, k:k + 1], min_val=0, max_val=NE - 1)
                for c in range(KD):
                    sp.dma_start(W1[:, k, c, :], w1[bass.ds(e, 1), c * P:(c + 1) * P, :]
                                 .rearrange("e p f -> (e p) f")).then_inc(r_w, 16)
                sp.dma_start(W2[:, k, :, :].rearrange("p c d -> p (c d)"),
                             w2[bass.ds(e, 1), :, :].rearrange("e (p c) d -> (e p) (c d)", c=FC)).then_inc(r_w, 16)
                sp.dma_start(b1c[:, k, :], b1[bass.ds(e, 1), :].rearrange("e (p c) -> (e p) c", c=FC)
                             ).then_inc(r_w, 16)
                sp.dma_start(b2row[0:1, k, :], b2[bass.ds(e, 1), :]).then_inc(r_w, 16)

            def store(s, u, i, do):
                sp.wait_ge(f_o, s + 1)
                sp.dma_start(out[bass.ds(s * P, P), :], fo[:, u % 2, :]).then_inc(f_out[u % 2], 16)
            pipeline(sp, LASTB, 2, 0, store)
            sp.wait_ge(f_o, LASTB + 1)
            sp.dma_start(out[LASTB * P:N, :], fo[0:TAIL, LASTB % 2, :]).then_inc(f_out[LASTB % 2], 16)
            for o in range(2):
                sp.wait_ge(f_out[o], 16 * len(range(o, LASTB + 1, 2)))

        @block.gpsimd
        def _(pool):
            nc.gpsimd.memset(ones[:], 1.0).then_inc(s_const, 1)
            nc.gpsimd.memset(onesb[:], 1.0).then_inc(s_const, 1)
            nc.gpsimd.memset(ident[:], 0.0).then_inc(s_iden, 1)
            pool.wait_ge(s_iden, 1)
            nc.gpsimd.affine_select(out=ident[:], in_=ident[:], compare_op=ALU.not_equal, fill=1.0, base=0,
                                    pattern=[[-1, P]], channel_multiplier=1).then_inc(s_iden, 1)
            pool.wait_ge(s_iden, 2)
            nc.gpsimd.tensor_copy(identb[:], ident[:]).then_inc(s_const, 1)
            nc.gpsimd.iota(iota[:], pattern=[[1, P]], base=0, channel_multiplier=0,
                           allow_small_or_imprecise_dtypes=True).then_inc(s_const, 1)
            nc.gpsimd.iota(blockbase[:], pattern=[[P, NB]], base=0, channel_multiplier=0,
                           allow_small_or_imprecise_dtypes=True).then_inc(s_const, 1)
            nc.gpsimd.iota(gidx[:], pattern=[[P, 4]], base=0, channel_multiplier=1).then_inc(s_const, 1)
            nc.gpsimd.iota(steps[:], pattern=[[1, SP_LEN]], base=0, channel_multiplier=0,
                           allow_small_or_imprecise_dtypes=True).then_inc(s_const, 1)
            nc.gpsimd.iota(rank[:], pattern=[[-1, NE]], base=NE, channel_multiplier=0,
                           allow_small_or_imprecise_dtypes=True).then_inc(s_const, 1)
            nc.gpsimd.memset(pathf[:], 1e9).then_inc(s_const, 1)
            nc.gpsimd.memset(neghalf[:], -0.5).then_inc(s_const, 1)

            def rstd(v, done):
                nc.gpsimd.tensor_tensor(small[:, v, 10:11], small[:, v, 8:9], neghalf[:], ALU.pow).then_inc(done, 1)

            def nodes(s, u, i, do):
                pool.wait_ge(s_st, s * 3 + 3)
                rstd(u % 2, s_rs)
            pipeline(pool, NB, 2, 0, nodes)
            pool.wait_ge(s_elm, 1)
            nc.gpsimd.partition_all_reduce(elmax[:, 1, :], elmax[:, 0, :], P,
                                           bass.bass_isa.ReduceOp.max).then_inc(s_gmax, 1)
            pool.wait_ge(s_tab, STORES * 16)

            def gather(s, u, i, do):
                pool.wait_ge(e_idx, s + 1)
                if do(U):
                    pool.wait_ge(e_sc, s - (U - 1))
                pool.sem_inc(s_held, 1)
                for j in range(TPG):
                    nc.gpsimd.indirect_dma_start(
                        out=gath[:, u, j, :], out_offset=None, in_=table[:, :],
                        in_offset=bass.IndirectOffsetOnAxis(ap=idx[:, u * TPG + j:u * TPG + j + 1], axis=0),
                    ).then_inc(e_gath[u], 16)
            pipeline(pool, STEPS, U, 0, gather)

            def residual(s, u, i, do):
                if do(0):
                    pool.wait_ge(n_hout, s + 1)
                    nc.gpsimd.tensor_tensor(blk(X, s), blk(X, s), blk(A, s), ALU.add).then_inc(n_x1, 1)
                if do(1):
                    pool.wait_ge(n_st, s * 3)
                    rstd(1 - u % 2, n_rs)
            pipeline(pool, NB, 2, 1, residual)

            def ffn_rstd(s, u, do):
                for t in range(CH):
                    pool.wait_ge(f_st, (s * CH + t) * 7 + 4)
                    rstd(t, f_rs)
            chunks(pool, ffn_rstd)

        @block.scalar
        def _(act):
            act.dma_start(ab[:], attn_w.rearrange("h d -> (h d)").partition_broadcast(P)).then_inc(s_ab, 16)
            act.dma_start(gam[:], gamma.partition_broadcast(P)).then_inc(r_gb, 16)
            act.dma_start(bet[:], beta.partition_broadcast(P)).then_inc(r_gb, 16)
            firstv = dst[0:1, :].rearrange("o (g j) -> (o g) j", j=TPG)
            with nc.allow_non_contiguous_dma(reason="one element of each group"):
                for c in range(4):
                    n = min(P, G - c * P)
                    act.dma_start(firsts[0:n, c:c + 1], firstv[c * P:c * P + n, 0:1]).then_inc(s_edges, 16)
            act.dma_start(srcs[:], src).then_inc(s_edges, 16)
            act.dma_start(dsts[:], dst).then_inc(s_edges, 16)
            act.dma_start(Wr[:], wr.rearrange("(k p) e -> p k e", p=P)).then_inc(r_gb, 16)
            act.dma_start(r8[0:1, 0, :], br.rearrange("(a e) -> a e", a=1)).then_inc(r_gb, 16)

            def nodes(s, u, i, do):
                v = u % 2
                if do(0):
                    act.wait_ge(s_hT, s + 1)
                    if do(2):
                        act.wait_ge(s_z, s - 1)
                    nc.scalar.activation(HT[:, v, :, :], bank[v][:, 0:D].rearrange("p (k n) -> p k n", k=KD),
                                         ACT.Copy).then_inc(s_hTc, 1)
                if do(1):
                    act.wait_ge(s_z, s)
                    nc.scalar.activation(blk(ee, s - 1, 0, 2 * H), bank[3 - v][:, D:D + 2 * H], ACT.Copy
                                         ).then_inc(s_ec, 1)
                    nc.scalar.activation(blk(A, s - 1, 0, ROW), bank[3 - v][:, 0:ROW], ACT.Copy).then_inc(s_zc, 1)
            def nodes_(s, u, i, do):
                nodes(s, u, i, (lambda lag: lag > 0) if isinstance(s, int) and s >= NB else do)
            pipeline(act, NB, 2, 1, nodes_)

            act.wait_ge(s_plan, 1)
            act.wait_ge(s_edges, 6 * 16)

            def edges(s, u, i, do):
                if do(0):
                    g = act.value_load(stepg[0:1, 0, bass.ds(s, 1)], min_val=0, max_val=G - 1)
                    if do(U):
                        act.wait_ge(e_gath[u], i * (TPG * 16))
                    nc.scalar.copy(idx[:, u * TPG:(u + 1) * TPG], srcs[:, bass.ds(g * TPG, TPG)]).then_inc(e_idx, 1)
                if do(LA):
                    t, w = s - LA, (u - LA) % U
                    act.wait_ge(e_oh, t + 1)
                    if do(LA + 4):
                        act.wait_ge(e_sc, t - 3)
                    nc.scalar.activation(OHf[:, w % 4, :, :], OHb[:, w % 2, :, :], ACT.Copy).then_inc(e_ohf, 1)
                    act.wait_ge(e_tp, t + 1)
                    if do(LA + 2):
                        act.wait_ge(e_er, t - 1)
                    nc.scalar.activation(OHT[:, w % 2, :, :], psT[w % 2], ACT.Copy).then_inc(e_ohT, 1)
                if do(LA + 1):
                    t, w = s - (LA + 1), (u - LA - 1) % U
                    act.wait_ge(e_lg, t + 1)
                    nc.scalar.activation(gath[:, w, :, D:ROW],
                                         logit[:, w % 2, 3, :].rearrange("p (j h) -> p j h", h=H),
                                         ACT.Exp).then_inc(e_num, 1)
            pipeline(act, STEPS, U, LA + 1, edges)

            def norm(s, u, i, do):
                v = u % 2
                if do(0):
                    act.wait_ge(n_bias, s + 1)
                    if do(2):
                        act.wait_ge(n_tp, s - 1)
                        act.wait_ge(n_keep, s - 1)
                    nc.scalar.activation(Hn[:, v, :], blk(X, s), ACT.Identity, bias=small[:, v, 11:12],
                                         scale=small[:, v, 10:11]).then_inc(n_xn, 1)
                if do(1):
                    act.wait_ge(n_tp, s)
                    nc.scalar.activation(XT[:, :, bass.ds((s - 1) * P, P)],
                                         bank[1 - v][:, 0:D].rearrange("p (k n) -> p k n", k=KD),
                                         ACT.Copy).then_inc(n_xT, 1)
            pipeline(act, NB, 2, 1, norm)

            for n, (o, a) in enumerate(((4, 3), (13, 12), (21, 20))):
                act.wait_ge(r_act, n + 1)
                nc.scalar.activation(r8[0:1, o, :], r8[0:1, a, :], ACT.Exp).then_inc(r_exp, 1)

            act.wait_ge(r_w, TOPK * 5 * 16)

            def gelu(s, u, do):
                if do(0):
                    for n in range(TOPK * FC):
                        act.wait_ge(f_h, s * (TOPK * FC) + (n + 1))
                        if n == 0 and do(2):
                            act.wait_ge(f_y, s * CH - CH)
                        nc.scalar.activation(hid[:, u % 2, n, :], bank[n % 4][:, 0:CH * P], ACT.Gelu,
                                             bias=b1c[:, n // FC, n % FC:n % FC + 1]).then_inc(f_g, 1)
            chunks(act, gelu)

        @block.tensor
        def _(pe):
            pe.wait_ge(s_const, 10)
            pe.wait_ge(s_wz, 1)

            def nodes(s, u, i, do):
                v = u % 2
                if do(0):
                    pe.wait_ge(s_h, s + 1)
                    if do(2):
                        pe.wait_ge(s_hTc, s - 1)
                    for k in range(KD):
                        last = nc.tensor.transpose(bank[v][:, k * P:(k + 1) * P], Hn[:, v, k * P:(k + 1) * P],
                                                   ident[:])
                    last.then_inc(s_hT, 1)
                if do(1):
                    pe.wait_ge(s_hTc, s)
                    if do(3):
                        pe.wait_ge(s_zc, s - 2)
                        pe.wait_ge(s_ec, s - 2)
                    for k in range(KD):
                        last = nc.tensor.matmul(bank[3 - v][:, 0:D + 2 * H], HT[:, 1 - v, k, :], Wz[:, k, :],
                                                start=(k == 0), stop=(k == KD - 1))
                    last.then_inc(s_z, 1)
            pipeline(pe, NB, 2, 1, nodes)

            pe.wait_ge(s_pass, 1)
            for c in range(4):
                last = nc.tensor.matmul(bank[4][0:1, 0:SP_LEN], onesb[:], passed[:, c, :], start=(c == 0), stop=(c == 3))
            last.then_inc(s_cnt, 1)

            pe.wait_ge(s_erc, 1)
            pe.wait_ge(s_plan, 1)

            def edges(s, u, i, do):
                if do(1):
                    t, v = s - 1, (u - 1) % 2
                    b = pe.value_load(stepg[0:1, 1, bass.ds(t, 1)], min_val=0, max_val=NB - 1)
                    pe.wait_ge(e_ohT, t + 1)
                    if do(3):
                        pe.wait_ge(e_l3, t - 1)
                    for j in range(TPG):
                        for q in range(3):
                            last = nc.tensor.matmul(psE[v][:, j, :], OHT[:, v, j, :],
                                                    erc3[:, bass.ds(b, 1), q, :].rearrange("p a c -> p (a c)"),
                                                    start=(q == 0), stop=(q == 2))
                    last.then_inc(e_er, 1)
                if do(0):
                    v = u % 2
                    pe.wait_ge(e_oh, s + 1)
                    if do(2):
                        pe.wait_ge(e_ohT, s - 1)
                    for j in range(TPG):
                        last = nc.tensor.transpose(psT[v][:, j, :], OHb[:, v, j, :], identb[:])
                    last.then_inc(e_tp, 1)
                if do(3):
                    t, w = s - 3, (u - 3) % U
                    pe.wait_ge(e_ohf, t + 1)
                    pe.wait_ge(e_msg, t + 1)
                    if do(5):
                        pe.wait_ge(e_acc, t - 1)
                    for j in range(TPG):
                        last = nc.tensor.matmul(psA[w % 2], OHf[:, w % 4, j, :], gath[:, w, j, :],
                                                start=(j == 0), stop=(j == TPG - 1))
                    last.then_inc(e_sc, 1)
            pipeline(pe, STEPS, U, 3, edges)

            def turn(s, u, i, do):
                v = u % 2
                pe.wait_ge(n_xn, s + 1)
                if do(2):
                    pe.wait_ge(n_xT, s - 1)
                for k in range(KD):
                    last = nc.tensor.transpose(bank[v][:, k * P:(k + 1) * P], Hn[:, v, k * P:(k + 1) * P], ident[:])
                last.then_inc(n_tp, 1)
            pipeline(pe, NB, 2, 0, turn)

            pe.wait_ge(r_mean, 1)
            pe.wait_ge(r_gb, 4 * 16)
            for k in range(KD):
                last = nc.tensor.matmul(bank[6][0:1, 0:NE], meanT[:, k:k + 1], Wr[:, k, :], start=(k == 0), stop=(k == KD - 1))
            last.then_inc(r_pe, 1)
            pe.wait_ge(r_wrow, 1)
            nc.tensor.matmul(bank[7][:, 0:TOPK], ones[0:1, :], r8[0:1, 23, 0:TOPK], start=True, stop=True).then_inc(r_pe, 1)
            pe.wait_ge(r_b2, 1)
            nc.tensor.matmul(bank[6][:, 0:D], ones[0:1, :], b2mix[0:1, 1, :], start=True, stop=True).then_inc(r_pe, 1)
            pe.wait_ge(r_ready, 1)

            def ffn(s, u, do):
                if do(0):
                    for n in range(TOPK * FC):
                        e, f = n // FC, n % FC
                        if n >= 4:
                            pe.wait_ge(f_g, s * (TOPK * FC) + (n - 3))
                        elif do(1):
                            pe.wait_ge(f_g, s * (TOPK * FC) + (n - 3))
                        for k in range(KD):
                            last = nc.tensor.matmul(bank[n % 4][:, 0:CH * P], W1[:, e, k, f::FC],
                                                    XT[:, k, bass.ds(s * (CH * P), CH * P)],
                                                    start=(k == 0), stop=(k == KD - 1))
                        last.then_inc(f_h, 1)
                if do(1):
                    pe.wait_ge(f_g, s * (TOPK * FC))
                    for t in range(CH):
                        if do(3):
                            pe.wait_ge(f_r, s * CH + (t + 1 - 3 * CH))
                        for n in range(TOPK * FC):
                            last = nc.tensor.matmul(bank[4 + (u - 1) % 2 * CH + t][:, 0:D],
                                                    hid[:, (u - 1) % 2, n, t * P:(t + 1) * P], W2[:, n // FC, n % FC, :],
                                                    start=(n == 0), stop=(n == TOPK * FC - 1))
                        last.then_inc(f_y, 1)
            chunks(pe, ffn, 1)

        @block.vector
        def _(dve):
            chain = [0]

            def link(ins):
                chain[0] += 1
                ins.then_inc(s_v, 1)
                dve.wait_ge(s_v, chain[0])

            def add_eps(slot, stats, at):
                dve.wait_ge(stats, at)
                nc.vector.tensor_scalar(slot[:, 8:9], slot[:, 7:8], LN_EPS, None, ALU.add).then_inc(stats, 1)

            dve.wait_ge(s_in, KD * 16)
            dve.wait_ge(s_ab, 16)
            for k in range(KD):
                for side in range(2):
                    a = ab[:].rearrange("p (h t d) -> p h t d", h=H, t=2)[:, :, side, :]
                    link(nc.vector.tensor_tensor(wprod[:].rearrange("p (h d) -> p h d", h=H),
                                                 Wz[:, k, 0:D].rearrange("p (h d) -> p h d", h=H), a, ALU.mult))
                    link(nc.vector.tensor_reduce(Wz[:, k, D + side * H:D + (side + 1) * H],
                                                 wprod[:].rearrange("p (h d) -> p h d", h=H), AX.X, ALU.add))
            nc.vector.memset(r8[0:1, 1:24, :], 0.0).then_inc(s_wz, 1)

            dve.wait_ge(s_edges, 6 * 16)
            dve.wait_ge(s_const, 10)
            for c in range(4):
                n = min(P, G - c * P)
                nc.vector.tensor_scalar(fblk[0:n, c:c + 1], firsts[0:n, c:c + 1], 7, None,
                                        ALU.arith_shift_right).then_inc(s_v, 1)
            chain[0] += 4
            dve.wait_ge(s_v, chain[0])
            for c in range(4):
                n = min(P, G - c * P)
                nc.vector.tensor_tensor(pathf[0:n, c:c + 1], fblk[0:n, c:c + 1], gidx[0:n, c:c + 1], ALU.add
                                        ).then_inc(s_v, 1)
            chain[0] += 4
            dve.wait_ge(s_v, chain[0])
            link(nc.vector.memset(pathf[0:1, 0:1], 1e9))
            for c in range(4):
                last = nc.vector.tensor_scalar(passed[:, c, :], steps[:], pathf[:, c:c + 1], None, ALU.is_ge)
            last.then_inc(s_pass, 1)

            dve.wait_ge(s_x, STORES * 16)

            def nodes(s, u, i, do):
                v = u % 2
                if do(0):
                    nc.vector.bn_stats(small[:, v, 0:6], blk(X, s)).then_inc(s_st, 1)
                    dve.wait_ge(s_st, s * 3 + 1)
                    dve.sem_inc(s_held, 1)
                    nc.vector.bn_aggr(small[:, v, 6:8], small[:, v, 0:6]).then_inc(s_st, 1)
                    add_eps(small[:, v, :], s_st, s * 3 + 2)
                if do(1):
                    w = 1 - v
                    dve.wait_ge(s_rs, s)
                    if do(3):
                        dve.wait_ge(s_hT, s - 2)
                    nc.vector.tensor_scalar(Hn[:, w, :], blk(X, s - 1), small[:, w, 6:7], small[:, w, 10:11],
                                            ALU.subtract, ALU.mult).then_inc(s_h, 1)
            pipeline(dve, NB, 2, 1, nodes)

            dve.wait_ge(s_ec, NB)
            nc.vector.tensor_reduce(elmax[:, 0, :], ee[:, :, 0:H].rearrange("p b h -> p h b"), AX.X, ALU.max
                                    ).then_inc(s_elm, 1)
            dve.wait_ge(s_cnt, 1)
            link(nc.vector.tensor_copy(stepf[0:1, 0, :], bank[4][0:1, 0:SP_LEN]))
            link(nc.vector.tensor_tensor(stepf[0:1, 1, :], steps[0:1, :], stepf[0:1, 0, :], ALU.subtract))
            link(nc.vector.tensor_scalar(stepf[0:1, 1, :], stepf[0:1, 1, :], float(NB - 1), None, ALU.min))
            nc.vector.tensor_copy(stepg[0:1, :, :], stepf[0:1, :, :]).then_inc(s_plan, 1)
            dve.wait_ge(s_gmax, 1)
            link(nc.vector.tensor_copy(erc[:, :, 0:H], ee[:, :, H:2 * H]))
            link(nc.vector.tensor_tensor(res[:, :, 0:H], ee[:, :, H:2 * H],
                                         elmax[:, 1:2, :].to_broadcast([P, NB, H]), ALU.add))
            link(nc.vector.scalar_tensor_tensor(out=erc[:, :, H:2 * H], in0=res[:, :, 0:H], scalar=SLOPE,
                                                in1=res[:, :, 0:H], op0=ALU.mult, op1=ALU.max))
            link(nc.vector.tensor_copy(erc3[:, :, 0, :], erc[:]))
            link(nc.vector.tensor_tensor(res[:], erc[:], erc3[:, :, 0, :], ALU.subtract))
            link(nc.vector.tensor_copy(erc3[:, :, 1, :], res[:]))
            link(nc.vector.tensor_tensor(erc[:], res[:], erc3[:, :, 1, :], ALU.subtract))
            nc.vector.tensor_copy(erc3[:, :, 2, :], erc[:]).then_inc(s_erc, 1)
            dve.wait_ge(s_tab, STORES * 16)
            link(nc.vector.memset(A[:], 0.0))
            dve.wait_ge(s_plan, 1)

            def edges(s, u, i, do):
                if do(0):
                    v = u % 2
                    g = dve.value_load(stepg[0:1, 0, bass.ds(s, 1)], min_val=0, max_val=G - 1)
                    b = dve.value_load(stepg[0:1, 1, bass.ds(s, 1)], min_val=0, max_val=NB - 1)
                    nc.vector.tensor_scalar(dloc[:, v, :], dsts[:, bass.ds(g * TPG, TPG)], blockbase[:, bass.ds(b, 1)],
                                            None, ALU.subtract).then_inc(e_dl, 1)
                if do(1):
                    t, w, r = s - 1, (u - 1) % U, i + (u - 1) // U
                    dve.wait_ge(e_er, t + 1)
                    dve.wait_ge(e_gath[w], r * (TPG * 16) + TPG * 16)
                    lg = [logit[:, w % 2, q, :].rearrange("p (j h) -> p j h", h=H) for q in range(4)]
                    if do(3):
                        dve.wait_ge(e_num, t - 1)
                    nc.vector.tensor_tensor(lg[0], gath[:, w, :, D:ROW], psE[w % 2][:, :, 0:H], ALU.add).then_inc(e_l1, 1)
                if do(0):
                    dve.wait_ge(e_dl, s + 1)
                    if do(2):
                        dve.wait_ge(e_tp, s - 1)
                        dve.wait_ge(e_ohf, s - 1)
                    for j in range(TPG):
                        last = nc.vector.tensor_scalar(OHb[:, v, j, :], iota[:], dloc[:, v, j:j + 1], None, ALU.is_equal)
                    last.then_inc(e_oh, 1)
                if do(1):
                    dve.wait_ge(e_l1, t + 1)
                    nc.vector.scalar_tensor_tensor(out=lg[1], in0=lg[0], scalar=SLOPE, in1=lg[0],
                                                   op0=ALU.mult, op1=ALU.max).then_inc(e_l2, 1)
                if do(4):
                    t4, w4 = s - 4, (u - 4) % U
                    b4 = dve.value_load(stepg[0:1, 1, bass.ds(t4, 1)], min_val=0, max_val=NB - 1)
                    dve.wait_ge(e_sc, t4 + 1)
                    if do(5):
                        dve.wait_ge(e_acc, t4)
                    nc.vector.tensor_tensor(blk(A, b4, 0, ROW), blk(A, b4, 0, ROW), psA[w4 % 2], ALU.add
                                            ).then_inc(e_acc, 1)
                if do(1):
                    dve.wait_ge(e_l2, t + 1)
                    nc.vector.tensor_tensor(lg[2], lg[1], psE[w % 2][:, :, H:2 * H], ALU.subtract).then_inc(e_l3, 1)
                if do(2):
                    t2, w2 = s - 2, (u - 2) % U
                    dve.wait_ge(e_num, t2 + 1)
                    z = gath[:, w2, :, 0:D].rearrange("p j (h d) -> p j h d", h=H)
                    nc.vector.tensor_tensor(z, z, gath[:, w2, :, D:ROW].unsqueeze(3).to_broadcast([P, TPG, H, HD]),
                                            ALU.mult).then_inc(e_msg, 1)
                if do(1):
                    dve.wait_ge(e_l3, t + 1)
                    nc.vector.tensor_scalar(lg[3], lg[2], 0.0, None, ALU.min).then_inc(e_lg, 1)
            pipeline(dve, STEPS, U, 4, edges)

            dve.wait_ge(e_acc, STEPS)
            link(nc.vector.scalar_tensor_tensor(out=rden[:], in0=A[:, :, D:ROW], scalar=0.0, in1=A[:, :, D:ROW],
                                                op0=ALU.is_equal, op1=ALU.add))
            link(nc.vector.reciprocal(rden[:], rden[:]))

            def finish(s, u, i, do):
                v = u % 2
                if do(0):
                    a = blk(A, s).rearrange("p (h d) -> p h d", h=H)
                    nc.vector.tensor_tensor(a, a, blk(rden, s, 0, H).unsqueeze(2).to_broadcast([P, H, HD]), ALU.mult
                                            ).then_inc(n_hout, 1)
                if do(1):
                    w = 1 - v
                    dve.wait_ge(n_x1, s)
                    if do(3):
                        dve.wait_ge(n_xn, s - 2)
                    nc.vector.bn_stats(small[:, w, 0:6], blk(X, s - 1)).then_inc(n_st, 1)
                    dve.wait_ge(n_st, s * 3 - 2)
                    dve.sem_inc(s_held, 1)
                    nc.vector.bn_aggr(small[:, w, 6:8], small[:, w, 0:6]).then_inc(n_st, 1)
                    add_eps(small[:, w, :], n_st, s * 3 - 1)
                if do(2):
                    dve.wait_ge(n_rs, s - 1)
                    nc.vector.scalar_tensor_tensor(out=small[:, v, 11:12], in0=small[:, v, 6:7], scalar=-1.0,
                                                   in1=small[:, v, 10:11], op0=ALU.mult, op1=ALU.mult
                                                   ).then_inc(n_bias, 1)
                if do(3):
                    dve.wait_ge(n_xn, s - 2)
                    nc.vector.tensor_copy(blk(A, s - 3), Hn[:, 1 - v, :]).then_inc(n_keep, 1)
            pipeline(dve, NB, 2, 3, finish)

            dve.wait_ge(n_xT, NB)
            link(nc.vector.tensor_reduce(meanT[:], XT[:, :, 0:N], AX.X, ALU.add))
            nc.vector.tensor_scalar(meanT[:], meanT[:], 1.0 / N, None, ALU.mult).then_inc(r_mean, 1)

            def R(n, w=NE):
                return r8[0:1, n, 0:w]

            dve.wait_ge(r_gb, 4 * 16)
            dve.wait_ge(r_pe, 1)
            link(nc.vector.tensor_tensor(R(1), bank[6][0:1, 0:NE], R(0), ALU.add))
            link(nc.vector.tensor_reduce(R(2, 1), R(1), AX.X, ALU.max))
            nc.vector.tensor_scalar(R(3), R(1), R(2, 1), None, ALU.subtract).then_inc(r_act, 1)
            dve.wait_ge(r_exp, 1)
            link(nc.vector.tensor_reduce(R(5, 1), R(4), AX.X, ALU.add))
            link(nc.vector.reciprocal(R(5, 1), R(5, 1)))
            link(nc.vector.tensor_scalar(R(6), R(4), R(5, 1), None, ALU.mult))
            link(nc.vector.tensor_scalar(R(7), R(6), float(N), None, ALU.mult))
            link(nc.vector.tensor_scalar(R(8), R(7), CAP, None, ALU.is_gt))
            link(nc.vector.reciprocal(R(9), R(7)))
            link(nc.vector.tensor_scalar(R(9), R(9), CAP, None, ALU.mult))
            link(nc.vector.tensor_tensor(R(9), R(9), R(8), ALU.mult))
            link(nc.vector.tensor_scalar(R(10), R(8), -1.0, 1.0, ALU.mult, ALU.add))
            link(nc.vector.tensor_tensor(R(9), R(9), R(10), ALU.add))
            link(nc.vector.tensor_tensor(R(9), R(9), R(6), ALU.mult))
            link(nc.vector.tensor_reduce(R(11, 1), R(9), AX.X, ALU.max))
            nc.vector.tensor_scalar(R(12), R(9), R(11, 1), None, ALU.subtract).then_inc(r_act, 1)
            dve.wait_ge(r_exp, 2)
            link(nc.vector.tensor_reduce(R(14, 1), R(13), AX.X, ALU.add))
            link(nc.vector.reciprocal(R(14, 1), R(14, 1)))
            link(nc.vector.tensor_scalar(R(15), R(13), R(14, 1), None, ALU.mult))
            for k in range(TOPK):
                link(nc.vector.tensor_reduce(R(16 + k, 1), R(15), AX.X, ALU.max))
                link(nc.vector.scalar_tensor_tensor(out=R(18), in0=R(15), scalar=R(16 + k, 1), in1=rank[0:1, :],
                                                    op0=ALU.is_equal, op1=ALU.mult))
                link(nc.vector.tensor_reduce(R(19, 1), R(18), AX.X, ALU.max))
                link(nc.vector.tensor_scalar(r8[0:1, 22, k:k + 1], R(19, 1), -1.0, float(NE), ALU.mult, ALU.add))
                link(nc.vector.tensor_scalar(R(18), R(18), R(19, 1), -2.0, ALU.is_equal, ALU.mult))
                link(nc.vector.tensor_tensor(R(15), R(15), R(18), ALU.add))
            nc.vector.tensor_copy(topi[0:1, :], r8[0:1, 22, 0:TOPK]).then_inc(r_top, 1)
            link(nc.vector.tensor_tensor(r8[0:1, 20, 1:2], R(17, 1), R(16, 1), ALU.subtract))
            nc.vector.memset(r8[0:1, 20, 0:1], 0.0).then_inc(r_act, 1)
            dve.wait_ge(r_exp, 3)
            link(nc.vector.tensor_reduce(R(19, 1), R(21, TOPK), AX.X, ALU.add))
            link(nc.vector.reciprocal(R(19, 1), R(19, 1)))
            nc.vector.tensor_scalar(R(23, TOPK), R(21, TOPK), R(19, 1), None, ALU.mult).then_inc(r_wrow, 1)
            dve.wait_ge(r_wrow, 1)
            dve.wait_ge(r_pe, 2)
            link(nc.vector.tensor_copy(wcol[:], bank[7][:, 0:TOPK]))
            dve.wait_ge(r_w, TOPK * 5 * 16)
            link(nc.vector.tensor_scalar(b2mix[0:1, 0, :], b2row[0:1, 0, :], r8[0:1, 23, 0:1], None, ALU.mult))
            nc.vector.scalar_tensor_tensor(out=b2mix[0:1, 1, :], in0=b2row[0:1, 1, :], scalar=r8[0:1, 23, 1:2],
                                           in1=b2mix[0:1, 0, :], op0=ALU.mult, op1=ALU.add).then_inc(r_b2, 1)
            for k in range(TOPK):
                w = W2[:, k, :, :].rearrange("p c d -> p (c d)")
                link(nc.vector.tensor_scalar(w, w, wcol[:, k:k + 1], None, ALU.mult))
            dve.wait_ge(r_pe, 3)
            nc.vector.tensor_copy(b2all[:], bank[6][:, 0:D]).then_inc(r_ready, 1)
            dve.wait_ge(r_ready, 1)

            def last_norm(s, u, do):
                if do(2):
                    for t in range(CH):
                        n = s * CH + (t - 2 * CH)
                        ps = bank[4 + (u - 2) % 2 * CH + t][:, 0:D]
                        q, f = small[:, t, :], fo[:, t, :]
                        dve.wait_ge(f_y, n + 1)
                        if do(3) or t:
                            dve.wait_ge(f_o, n)
                        nc.vector.tensor_tensor(rbuf[:, 0, :], ps, blk(A, n), ALU.add).then_inc(f_r, 1)
                        dve.wait_ge(f_r, n + 1)
                        nc.vector.tensor_tensor(rbuf[:, 1, :], rbuf[:, 0, :], b2all[:], ALU.add).then_inc(f_st, 1)
                        dve.wait_ge(f_st, n * 7 + 1)
                        nc.vector.bn_stats(q[:, 0:6], rbuf[:, 1, :]).then_inc(f_st, 1)
                        dve.wait_ge(f_st, n * 7 + 2)
                        dve.sem_inc(s_held, 1)
                        nc.vector.bn_aggr(q[:, 6:8], q[:, 0:6]).then_inc(f_st, 1)
                        add_eps(q, f_st, n * 7 + 3)
                        dve.wait_ge(f_rs, n + 1)
                        nc.vector.tensor_scalar(rbuf[:, 0, :], rbuf[:, 1, :], q[:, 6:7], q[:, 10:11], ALU.subtract,
                                                ALU.mult).then_inc(f_st, 1)
                        dve.wait_ge(f_st, n * 7 + 5)
                        nc.vector.tensor_tensor(rbuf[:, 1, :], rbuf[:, 0, :], gam[:], ALU.mult).then_inc(f_st, 1)
                        dve.wait_ge(f_st, n * 7 + 6)
                        nc.vector.tensor_tensor(rbuf[:, 0, :], rbuf[:, 1, :], xb_(n), ALU.add).then_inc(f_st, 1)
                        dve.wait_ge(f_st, n * 7 + 7)
                        if do(3):
                            dve.wait_ge(f_out[t], s * 16 - 2 * 16)
                        nc.vector.tensor_tensor(f, rbuf[:, 0, :], bet[:], ALU.add).then_inc(f_o, 1)

            def xb_(n):
                return blk(X, n)
            chunks(dve, last_norm, 2)


_INS = ["x", "src", "dst", "gnn_w", "attn_w", "wr", "br", "w1", "b1", "w2", "b2", "gamma", "beta"]


def kernel(x, src, dst, L0_gnn_W, L0_gnn_attn_w, L0_ffn_Wr, L0_ffn_br, L0_ffn_W1, L0_ffn_b1, L0_ffn_W2, L0_ffn_b2,
           L0_ffn_gamma, L0_ffn_beta):
    import numpy as np
    import concourse.bacc as bacc
    from concourse.bass_utils import run_bass_kernel_spmd

    def grouped(a, fill):
        a = np.pad(np.asarray(a), (0, G * GE - E), constant_values=fill)
        return np.ascontiguousarray(a.reshape(G, TPG, P).transpose(2, 0, 1).reshape(P, G * TPG))

    values = [np.pad(np.asarray(x), ((0, NODES - N), (0, 0)), mode="edge"),
              grouped(src, 0), grouped(dst, 2 * NODES),
              L0_gnn_W, L0_gnn_attn_w, L0_ffn_Wr, L0_ffn_br, L0_ffn_W1, L0_ffn_b1, L0_ffn_W2, L0_ffn_b2,
              L0_ffn_gamma, L0_ffn_beta]
    nc = bacc.Bacc("TRN2", target_bir_lowering=False, num_devices=1)
    arrays, args = {}, []
    for name, a in zip(_INS, values):
        a = np.ascontiguousarray(a)
        arrays[f"in_{name}"] = a
        args.append(nc.dram_tensor(f"in_{name}", a.shape, mybir.dt.from_np(a.dtype), kind="ExternalInput").ap())
    table = nc.dram_tensor("z_el_table", (NODES, ROW), F32, kind="Internal").ap()
    out = nc.dram_tensor("out_0", (N, D), F32, kind="ExternalOutput").ap()
    build(nc, *args, table, out)
    r = run_bass_kernel_spmd(nc, [arrays], core_ids=[0])
    return r.results[0]["out_0"]
```
